# Optimizing a Trainium2 kernel written in Bass

```python
import numpy as np
import jax
import jax.numpy as jnp

def _softmax(x, axis=-1):
    return jax.nn.softmax(x, axis=axis)

def _gelu(x):
    return jax.nn.gelu(x, approximate=True)

def _silu(x):
    return jax.nn.silu(x)

def _sigmoid(x):
    return jax.nn.sigmoid(x)

def _layernorm(x, axis=-1, eps=1e-05):
    m = jnp.mean(x, axis=axis, keepdims=True)
    v = jnp.var(x, axis=axis, keepdims=True)
    return (x - m) / jnp.sqrt(v + eps)

def _scatter_add(tgt, idx, src, axis=0):
    return tgt.at[idx].add(src)

def _segment_sum(src, seg, n):
    return jax.ops.segment_sum(src, seg, n)
kernel_name = 'mk_xattn_ffn_d1_seqx_r8_5beb38'

def setup_inputs(seed: int=0):
    np.random.seed(seed)
    _w = jnp.asarray

    def _rec_inputs():
        import jax
        import jax.numpy as jnp
        _rk = jax.random.key(seed)
        x = -0.0003929 + 0.9999 * jax.random.normal(jax.random.fold_in(_rk, 1), (4, 256, 512), jnp.float32)
        _lenS = 256 - jax.random.randint(jax.random.fold_in(_rk, 7), (4,), 0, max(1, 256 // 4) + 1, jnp.int32)
        _lenS2 = 64 - jax.random.randint(jax.random.fold_in(_rk, 8), (4,), 0, max(1, 64 // 4) + 1, jnp.int32)
        _ctx_1024P = jax.random.normal(jax.random.fold_in(_rk, 11), (4, 16, 128), jnp.float32)
        _ctx_1024c = jax.random.dirichlet(jax.random.fold_in(_rk, 511), 0.3 * jnp.ones((16,), jnp.float32), (4, 64))
        _ctx_1024t = jnp.einsum('bsk,bkd->bsd', _ctx_1024c, _ctx_1024P)
        _ctx_1024t = _ctx_1024t * jax.lax.rsqrt(jnp.mean(jnp.square(_ctx_1024t)) + 1e-12) * 0.953939
        ctx_1024 = -1.39393e-06 + 0.999914 * (_ctx_1024t + 0.3 * jax.random.normal(jax.random.fold_in(_rk, 611), (4, 64, 128), jnp.float32))
        _validS = jnp.arange(256)[None, :] < _lenS[:, None]
        _validS2 = jnp.arange(64)[None, :] < _lenS2[:, None]
        _causal = jnp.tril(jnp.ones((256, 256), dtype=bool))
        mask_SxS2_ff0 = jnp.where(jnp.ones((256, 64), dtype=bool), 0.0, -1000000000.0).astype(jnp.float32)
        return (x, ctx_1024, mask_SxS2_ff0)
    x, ctx_1024, mask_SxS2_ff0 = _rec_inputs()

    def _L0_xattn_setup():
        import math
        import jax, jax.numpy as jnp
        import numpy as np
        N_HEADS = 32
        N_KV_HEADS = 8
        N_REP = N_HEADS // N_KV_HEADS
        HEAD_DIM = 512 // N_HEADS
        key = jax.random.key(seed)
        kq, kk, kv = jax.random.split(key, 3)
        B, S, T = (2, 256, 256)
        q = jax.random.normal(kq, (B, S, N_HEADS * HEAD_DIM), dtype=jnp.float32)
        k = jax.random.normal(kk, (B, T, N_KV_HEADS * HEAD_DIM), dtype=jnp.float32)
        v = jax.random.normal(kv, (B, T, N_KV_HEADS * HEAD_DIM), dtype=jnp.float32)
        mask = jnp.zeros((S, T), dtype=jnp.float32)
        return {'q': q, 'k': k, 'v': v, 'start_pos': 0, 'mask': mask}
    _L0_xattn_all = _L0_xattn_setup()
    _L0_xattn_in = {k: v for k, v in _L0_xattn_all.items() if k in ()}
    del _L0_xattn_all

    def _L0_ffn_setup():
        import jax, jax.numpy as jnp
        import numpy as np
        BS = 128
        FP8_MAX = 448.0

        def act_quant(x):
            T, K = x.shape
            xb = x.reshape(T, K // BS, BS)
            amax = jnp.max(jnp.abs(xb), axis=-1)
            scale = amax / FP8_MAX + 1e-12
            xq = (xb / scale[:, :, None]).reshape(T, K)
            return (xq, scale)

        def linear_dsv3(x, wq, w_scale):
            T, K = x.shape
            N = wq.shape[0]
            xq, xs = act_quant(x)
            xdq = (xq.reshape(T, K // BS, BS) * xs[:, :, None]).reshape(T, K)
            wdq = (wq.reshape(N // BS, BS, K // BS, BS) * w_scale[:, None, :, None]).reshape(N, K)
            return xdq @ wdq.T
        key = jax.random.key(seed)
        ks = jax.random.split(key, 4)
        DIM, INTER = (512, 1792)

        def make_qweight(k, n, m):
            w = jax.random.normal(k, (n, m), dtype=jnp.float32) * 0.02
            wb = w.reshape(n // BS, BS, m // BS, BS)
            amax = jnp.max(jnp.abs(wb), axis=(1, 3))
            scale = amax / FP8_MAX + 1e-12
            wq = (wb / scale[:, None, :, None]).reshape(n, m)
            return (wq, scale)
        x = jax.random.normal(ks[0], (2, 128, DIM), dtype=jnp.float32)
        w1, w1_scale = make_qweight(ks[1], INTER, DIM)
        w3, w3_scale = make_qweight(ks[2], INTER, DIM)
        w2, w2_scale = make_qweight(ks[3], DIM, INTER)
        return {'x': x, 'w1': w1, 'w1_scale': w1_scale, 'w3': w3, 'w3_scale': w3_scale, 'w2': w2, 'w2_scale': w2_scale}
    _L0_ffn_all = _L0_ffn_setup()
    _L0_ffn_in = {k: v for k, v in _L0_ffn_all.items() if k in ('w1', 'w1_scale', 'w3', 'w3_scale', 'w2', 'w2_scale')}
    del _L0_ffn_all
    return {'x': x, 'ctx_1024': ctx_1024, 'mask_SxS2_ff0': mask_SxS2_ff0, 'L0_ffn_w1': _L0_ffn_in['w1'], 'L0_ffn_w1_scale': _L0_ffn_in['w1_scale'], 'L0_ffn_w3': _L0_ffn_in['w3'], 'L0_ffn_w3_scale': _L0_ffn_in['w3_scale'], 'L0_ffn_w2': _L0_ffn_in['w2'], 'L0_ffn_w2_scale': _L0_ffn_in['w2_scale']}

def reference(x, ctx_1024, mask_SxS2_ff0, L0_ffn_w1, L0_ffn_w1_scale, L0_ffn_w3, L0_ffn_w3_scale, L0_ffn_w2, L0_ffn_w2_scale):
    import jax
    import jax.numpy as jnp

    def _L0_xattn_ref(q, k, v, start_pos, mask):
        import math
        import jax, jax.numpy as jnp
        import numpy as np
        N_HEADS = 32
        N_KV_HEADS = 8
        N_REP = N_HEADS // N_KV_HEADS
        HEAD_DIM = 512 // N_HEADS
        b, s, _ = q.shape
        t = k.shape[1]
        xq = q.reshape(b, s, N_KV_HEADS, N_REP, HEAD_DIM)
        xk = k.reshape(b, t, N_KV_HEADS, HEAD_DIM)
        xv = v.reshape(b, t, N_KV_HEADS, HEAD_DIM)
        scores = jnp.einsum('bsgrd,btgd->bgrst', xq, xk) / math.sqrt(HEAD_DIM)
        scores = scores + mask
        probs = jax.nn.softmax(scores.astype(jnp.float32), axis=-1).astype(q.dtype)
        out = jnp.einsum('bgrst,btgd->bsgrd', probs, xv)
        return out.reshape(b, s, N_HEADS * HEAD_DIM)

    def _L0_ffn_ref(x, w1, w1_scale, w3, w3_scale, w2, w2_scale):
        import jax, jax.numpy as jnp
        import numpy as np
        BS = 128
        FP8_MAX = 448.0

        def act_quant(x):
            T, K = x.shape
            xb = x.reshape(T, K // BS, BS)
            amax = jnp.max(jnp.abs(xb), axis=-1)
            scale = amax / FP8_MAX + 1e-12
            xq = (xb / scale[:, :, None]).reshape(T, K)
            return (xq, scale)

        def linear_dsv3(x, wq, w_scale):
            T, K = x.shape
            N = wq.shape[0]
            xq, xs = act_quant(x)
            xdq = (xq.reshape(T, K // BS, BS) * xs[:, :, None]).reshape(T, K)
            wdq = (wq.reshape(N // BS, BS, K // BS, BS) * w_scale[:, None, :, None]).reshape(N, K)
            return xdq @ wdq.T
        B, S, D = x.shape
        xf = x.reshape(-1, D)
        g = linear_dsv3(xf, w1, w1_scale)
        u = linear_dsv3(xf, w3, w3_scale)
        h = jax.nn.silu(g) * u
        y = linear_dsv3(h, w2, w2_scale)
        return y.reshape(B, S, D)
    x = x + _L0_xattn_ref(_layernorm(x, axis=-1), ctx_1024, ctx_1024, 0, mask_SxS2_ff0)
    x = x + _L0_ffn_ref(_layernorm(x, axis=-1), L0_ffn_w1, L0_ffn_w1_scale, L0_ffn_w3, L0_ffn_w3_scale, L0_ffn_w2, L0_ffn_w2_scale)
    return x

_drawn_inputs = setup_inputs


def setup_inputs(seed=0):
    import zlib

    import numpy as np

    out = dict(_drawn_inputs(seed))
    spreads = {'mask_SxS2_ff0': (0.0, 0.649)}
    factors = {'L0_ffn_w1_scale': 8.0, 'L0_ffn_w3_scale': 8.0, 'L0_ffn_w2_scale': 8.0}
    for name, (base, spread) in spreads.items():
        noise = np.random.default_rng([zlib.crc32(name.encode()), seed]).standard_normal(out[name].shape)
        drawn = base * np.exp(spread * noise) if base else spread * noise
        out[name] = jnp.asarray(drawn.astype(out[name].dtype))
    for name, factor in factors.items():
        out[name] = (out[name] * factor).astype(out[name].dtype)
    return out
```

```python
from contextlib import ExitStack

import numpy as np

import concourse.bass as bass
from concourse import mybir

F32 = mybir.dt.float32
F32R = mybir.dt.float32r
I32 = mybir.dt.int32
ALU = mybir.AluOpType
ACT = mybir.ActivationFunctionType
AX = mybir.AxisListType

P = 128
B, S, T, D, INTER = 4, 256, 64, 512, 1792
OCTS = D // P
GROUPS = 8
HALVES = T // 32
TB = S // 32
BLOCK = 2 * S
CHUNKS = INTER // P
STEPS = CHUNKS // 2
SLOTS = 3 * STEPS
UNITS = 3 * CHUNKS
RING = 7
STAGE = 3
AHEAD = 3
SEEDS = 3
EPS = 1e-5
RSQRT_MAGIC = float(0x5F3759DF)


FRONT = [5, 6, 8, 9, 11, 12, 14, 15]
BACK, VALUES = 1, 2
MEAN1, VAR1 = 1, 3
SUM2, MEAN2, VAR2 = 17, 18, 20


def group_in(slot, shift):
    return FRONT.index(slot - shift) if slot - shift in FRONT else None


def build(nc, xq, xr, kd, vd, mask, sel, scales, w1, w3, w2, out):
    with ExitStack() as ctx:
        def sb(name, shape, dt=F32):
            return ctx.enter_context(nc.sbuf_tensor(name, shape, dt))

        def sem(name):
            return ctx.enter_context(nc.semaphore(name))

        x_q = sb("x_q", [P, OCTS, S])
        res = [sb(f"res{k}", [P, OCTS, BLOCK]) for k in range(2)]
        xn_hi = [sb(f"xn_hi{k}", [P, OCTS, BLOCK], F32R) for k in range(2)]
        xn_lo = [sb(f"xn_lo{k}", [P, OCTS, BLOCK], F32R) for k in range(2)]
        keys = sb("keys", [P, GROUPS * HALVES, P])
        values_ = sb("values_", [P, GROUPS * HALVES, P])
        mask_raw = sb("mask_raw", [P, S])
        mask_split = sb("mask_split", [P, S], F32R)
        sel_raw = sb("sel_raw", [P, HALVES, P])
        sel_r = sb("sel_r", [P, HALVES, P], F32R)
        ones = sb("ones", [P, P])
        zeros = sb("zeros", [P, BLOCK], mybir.dt.bfloat16)
        fsum = sb("fsum", [P, 2, S])
        fsum1 = sb("fsum1", [P, S])
        xc = [sb(f"xc{k}", [P, OCTS, S]) for k in range(2)]
        xsq = sb("xsq", [P, OCTS, S])
        var8 = sb("var8", [P, TB])
        shifted = sb("shifted", [P, TB], I32)
        rs8 = sb("rs8", [P, TB])
        newton = sb("newton", [P, TB])
        rstd = sb("rstd", [P, S])
        max16 = sb("max16", [P, HALVES, TB])
        max8 = sb("max8", [P, TB])
        max_rows = sb("max_rows", [P, S])
        shifted_s = sb("shifted_s", [P, 2, HALVES, S])
        e = sb("e", [P, 2, HALVES, S])
        sum16 = sb("sum16", [P, 2, HALVES, TB])
        sum8 = sb("sum8", [P, 2, 2, TB])
        inv8 = sb("inv8", [P, 2, TB])
        inv_rows = sb("inv_rows", [P, S])
        att = sb("att", [P, S])
        w_raw = sb("w_raw", [P, STAGE, 4, P])
        w_hi = sb("w_hi", [P, RING, 4, P], F32R)
        w_lo = sb("w_lo", [P, RING, 4, P], F32R)
        scl = sb("scl", [P, CHUNKS + 1, 3, 4])
        th = sb("th", [P, BLOCK])
        tg = sb("tg", [P, BLOCK])
        h = sb("h", [P, 2, BLOCK])
        h_hi = sb("h_hi", [P, 2, BLOCK], F32R)
        h_lo = sb("h_lo", [P, 2, BLOCK], F32R)

        bank = [ctx.enter_context(nc.psum_tensor(f"bank{k}", [P, BLOCK], F32)) for k in range(8)]
        y_ps, g_ps, u_ps = bank[0:4], bank[4], bank[5]
        mean_ps = bank[7][:, S:2 * S]
        s_banks = {True: [bank[6], g_ps], False: [bank[6], bank[6]]}
        a_banks = {True: [bank[7], u_ps], False: [bank[7], bank[7]]}

        in_const = sem("in_const")
        in_xq = sem("in_xq")
        in_xr = [sem(f"in_xr{k}") for k in range(2)]
        in_k = sem("in_k")
        in_v = sem("in_v")
        in_w = [sem(f"in_w{k}") for k in range(STAGE)]
        out_done = sem("out_done")
        const_set = sem("const_set")
        const_act = sem("const_act")
        mask_done = sem("mask_done")
        scl_done = sem("scl_done")
        dve_link = sem("dve_link")
        ln_sum = sem("ln_sum")
        ln_stat = sem("ln_stat")
        ln_xc = sem("ln_xc")
        ln_sq = sem("ln_sq")
        ln_xn = sem("ln_xn")
        s_done = sem("s_done")
        s_taken = sem("s_taken")
        e_done = sem("e_done")
        e_summed = sem("e_summed")
        pv_done = sem("pv_done")
        a_taken = sem("a_taken")
        res_done = sem("res_done")
        xn_hi_done = sem("xn_hi_done")
        xn_lo_done = sem("xn_lo_done")
        wd_up_done = sem("wd_up_done")
        wd_down_done = sem("wd_down_done")
        w_hi_done = sem("w_hi_done")
        w_lo_done = sem("w_lo_done")
        g_done = sem("g_done")
        u_done = sem("u_done")
        y_step = sem("y_step")
        th_done = sem("th_done")
        tg_done = sem("tg_done")
        h_done = sem("h_done")
        h_hi_done = sem("h_hi_done")
        h_lo_done = sem("h_lo_done")
        y_taken = sem("y_taken")

        GU0, Y0 = 1, 2
        XN0 = 1
        LINKS_LN = 1 + 1 + 4 + 3 * SEEDS + 1 + 1
        LINKS = 2 * LINKS_LN + GROUPS * 4 + OCTS * 2

        def chunk(blk, i, j):
            return CHUNKS * blk + STEPS * i + j

        def unit_ahead(blk, i, slot):
            u = UNITS * blk + SLOTS * i + slot + AHEAD
            return u, not (isinstance(u, int) and u >= 2 * UNITS)

        block = ctx.enter_context(nc.Block())

        @block.sync
        def _(sp):
            def load_query(b):
                if b > 0:
                    sp.wait_ge(ln_xc, 2 * b - 1)
                sp.dma_start(x_q[:, :, :], xq[b, :, :, :]).then_inc(in_xq, 16)

            def load_keys_values(b):
                if b > 0:
                    sp.wait_ge(s_done, GROUPS * b)
                sp.dma_start(keys[:, :, :], kd[b, :, :, :]).then_inc(in_k, 16)
                if b > 0:
                    sp.wait_ge(pv_done, GROUPS * b)
                sp.dma_start(values_[:, :, :], vd[b, :, :, :]).then_inc(in_v, 16)

            def load_residual(b):
                sp.dma_start(res[b // 2][:, :, (b % 2) * S:(b % 2 + 1) * S], xr[b, :, :, :])\
                  .then_inc(in_xr[b // 2], 16)

            def load_unit(u):
                n, kind = u % UNITS // 3, u % 3
                if u >= STAGE:
                    sp.wait_ge(w_lo_done, u - STAGE + 1)
                sp.dma_start(w_raw[:, u % STAGE, :, :], [w1, w3, w2][kind][n, :, :, :])\
                  .then_inc(in_w[u % STAGE], 16)

            def store_block(blk):
                for o in range(OCTS):
                    sp.wait_ge(y_taken, OCTS * blk + o + 1)
                    sp.dma_start(out[blk, :, o, :], res[blk][:, o, :]).then_inc(out_done, 16)

            load_query(0)
            load_keys_values(0)
            sp.dma_start(mask_raw[:, :], mask).then_inc(in_const, 16)
            sp.dma_start(sel_raw[:, :, :], sel).then_inc(in_const, 16)
            sp.dma_start(scl[:, :, :, :], scales).then_inc(in_const, 16)
            load_residual(0)
            load_residual(1)
            for u in range(AHEAD):
                load_unit(u)
            load_query(1)
            load_keys_values(1)
            load_residual(2)
            load_residual(3)
            load_query(2)
            load_keys_values(2)
            for u in range(AHEAD, 2 * UNITS):
                load_unit(u)
                if u == SLOTS:
                    load_query(3)
                    load_keys_values(3)
                if u == UNITS + 2 * STAGE:
                    store_block(0)
            store_block(1)
            sp.wait_ge(out_done, 16 * 2 * OCTS)

        @block.tensor
        def _(pe):
            def stat(count):
                pe.wait_ge(ln_sum, count)
                pe.matmul(mean_ps, ones[:, :], fsum1[:, :], start=True, stop=True).then_inc(ln_stat, 1)

            def scores(b, g, two):
                n = GROUPS * b + g
                if g == 0:
                    pe.wait_ge(in_k, 16 * b + 16)
                    pe.wait_ge(ln_xn, 2 * b + 1)
                if g >= (2 if two else 1):
                    pe.wait_ge(s_taken, n - (1 if two else 0))
                dst = s_banks[two][g % 2]
                q = xc[0][:, g // 2, :]
                for half in range(HALVES):
                    d, k = dst[:, half * S:(half + 1) * S], HALVES * g + half
                    pe.matmul(d, sel_r[:, half, :], mask_split[:, :], start=True, stop=False)
                    last = pe.matmul(d, keys[:, k, :], q, start=False, stop=True)
                last.then_inc(s_done, 1)

            def values(b, g, two):
                n, o = GROUPS * b + g, g // 2
                if g == 0:
                    pe.wait_ge(in_v, 16 * b + 16)
                if g % 2 == 0 and o >= (2 if two else 1):
                    pe.wait_ge(a_taken, OCTS * b + o - (1 if two else 0))
                pe.wait_ge(e_done, n + 1)
                d = a_banks[two][o % 2][:, 0:S]
                for half in range(HALVES):
                    k = HALVES * g + half
                    last = pe.matmul(d, values_[:, k, :], e[:, g % 2, half, :], start=(g % 2 == 0 and half == 0),
                                     stop=(g % 2 == 1 and half == HALVES - 1))
                last.then_inc(pv_done, 1)

            def attention(b, slot, two):
                if slot == MEAN1:
                    stat(4 * b + 1)
                if slot == VAR1:
                    stat(4 * b + 2)
                g = group_in(slot, 0)
                if g is not None:
                    scores(b, g, two)
                g = group_in(slot, VALUES)
                if g is not None:
                    values(b, g, two)
                if slot == MEAN2:
                    stat(4 * b + 3)
                if slot == VAR2:
                    stat(4 * b + 4)

            def hidden_half(blk, i, j, kind):
                n, ring = chunk(blk, i, j), (3 * j + kind) % RING
                pe.wait_ge(w_hi_done, 3 * n + kind + 1)
                pe.wait_ge(w_lo_done, 3 * n + kind + 1)
                if j > 0:
                    pe.wait_ge([tg_done, h_done][kind], n)
                dst = [g_ps, u_ps][kind]
                for o in range(OCTS):
                    hi, lo = xn_hi[blk][:, o, :], xn_lo[blk][:, o, :]
                    pe.matmul(dst[:, :], w_hi[:, ring, o, :], hi, start=(o == 0), stop=False)
                    pe.matmul(dst[:, :], w_hi[:, ring, o, :], lo, start=False, stop=False)
                    last = pe.matmul(dst[:, :], w_lo[:, ring, o, :], hi, start=False, stop=(o == OCTS - 1))
                last.then_inc([g_done, u_done][kind], 1)

            def output_step(blk, i, j):
                n, ring = chunk(blk, i, j), (3 * j + 2) % RING
                pe.wait_ge(w_hi_done, 3 * n + 3)
                pe.wait_ge(w_lo_done, 3 * n + 3)
                pe.wait_ge(h_hi_done, n + 1)
                pe.wait_ge(h_lo_done, n + 1)
                hi, lo = h_hi[:, j % 2, :], h_lo[:, j % 2, :]
                for o in range(OCTS):
                    y = y_ps[o][:, :]
                    pe.matmul(y, w_hi[:, ring, o, :], hi, start=False, stop=False, skip_group_check=True)
                    pe.matmul(y, w_hi[:, ring, o, :], lo, start=False, stop=False, skip_group_check=True)
                    last = pe.matmul(y, w_lo[:, ring, o, :], hi, start=False, stop=False, skip_group_check=True)
                last.then_inc(y_step, 1)

            def seed(blk):
                for o in range(OCTS):
                    z = pe.matmul(y_ps[o][:, :], zeros[:, 0:P], zeros[:, :], start=True, stop=True,
                                  skip_group_check=True)
                    if blk == 0:
                        z.then_inc([y_step, y_step, g_done, u_done][o], 1)

            def ffn(blk, i, attend):
                for j in range(STEPS):
                    hidden_half(blk, i, j, 0)
                    if attend:
                        attention(2 + i, 3 * j, False)
                    hidden_half(blk, i, j, 1)
                    if attend:
                        attention(2 + i, 3 * j + 1, False)
                    if j > 0:
                        output_step(blk, i, j - 1)
                    if attend:
                        attention(2 + i, 3 * j + 2, False)
                output_step(blk, i, STEPS - 1)

            pe.wait_ge(const_set, 1)
            pe.wait_ge(const_act, 2)
            pe.wait_ge(mask_done, 1)
            with pe.Fori(0, 2) as b:
                for slot in range(SLOTS):
                    attention(b, slot, True)
            pe.wait_ge(xn_hi_done, 2)
            pe.wait_ge(xn_lo_done, 2 + XN0)
            seed(0)
            with pe.Fori(0, 2) as i:
                ffn(0, i, True)
            pe.wait_ge(xn_hi_done, 4)
            pe.wait_ge(xn_lo_done, 4 + XN0)
            pe.wait_ge(y_taken, OCTS)
            seed(1)
            with pe.Fori(0, 2) as i:
                ffn(1, i, False)

        @block.vector
        def _(dve):
            def attention(b, slot, k, off, two):
                n_links = [LINKS * b + links_before(slot)]
                stream = res[k][:, :, bass.ds(off, S)]

                def link(ins):
                    n_links[0] = n_links[0] + 1
                    ins.then_inc(dve_link, 1)
                    dve.wait_ge(dve_link, n_links[0])

                def octet_sums(src):
                    link(dve.tensor_tensor(fsum[:, :, :], src[:, 0:2, :], src[:, 2:4, :], ALU.add))
                    dve.tensor_tensor(fsum1[:, :], fsum[:, 0, :], fsum[:, 1, :], ALU.add).then_inc(ln_sum, 1)

                def centre(src, which):
                    dve.wait_ge(ln_stat, 4 * b + 2 * which + 1)
                    if which == 1:
                        dve.wait_ge(xn_lo_done, b + XN0)
                    dve.tensor_tensor(xc[which][:, :, :], src, mean_ps.unsqueeze(1).broadcast_to([P, OCTS, S]),
                                      ALU.subtract).then_inc(ln_xc, 1)

                def normalise(which, scale):
                    dve.wait_ge(ln_stat, 4 * b + 2 * which + 2)
                    link(dve.tensor_reduce(var8[:, :], mean_ps.rearrange("p (a b) -> p a b", b=32), AX.X, ALU.max,
                                           apply_transpose=True))
                    link(dve.tensor_scalar(var8[:, :], var8[:, :], EPS, None, ALU.add))
                    link(dve.tensor_scalar(shifted[:, :], var8[:, :].bitcast(I32), 1, None, ALU.logical_shift_right))
                    link(dve.tensor_scalar(rs8[:, :].bitcast(I32), shifted[:, :], -1.0, RSQRT_MAGIC,
                                           ALU.mult, ALU.add))
                    for _ in range(SEEDS):
                        link(dve.scalar_tensor_tensor(out=newton[:, :], in0=rs8[:, :], scalar=-0.5, in1=rs8[:, :],
                                                      op0=ALU.mult, op1=ALU.mult))
                        link(dve.tensor_tensor(newton[:, :], newton[:, :], var8[:, :], ALU.mult))
                        link(dve.scalar_tensor_tensor(out=rs8[:, :], in0=newton[:, :], scalar=1.5, in1=rs8[:, :],
                                                      op0=ALU.add, op1=ALU.mult))
                    link(dve.tensor_scalar(rs8[:, :], rs8[:, :], scale, None, ALU.mult))
                    link(dve.transpose(rstd[:, :].rearrange("p (a b) -> p a b", b=32),
                                       rs8[:, :].unsqueeze(2).broadcast_to([P, TB, 32])))
                    dve.tensor_tensor(xc[which][:, :, :], xc[which][:, :, :],
                                      rstd[:, :].unsqueeze(1).broadcast_to([P, OCTS, S]), ALU.mult).then_inc(ln_xn, 1)

                def front(g):
                    s = s_banks[two][g % 2][:, :]
                    dve.wait_ge(s_done, GROUPS * b + g + 1)
                    link(dve.tensor_reduce(max16[:, :, :].rearrange("p h j -> p (h j)"),
                                           s.rearrange("p (a b) -> p a b", b=32), AX.X, ALU.max,
                                           apply_transpose=True))
                    link(dve.tensor_tensor(max8[:, :], max16[:, 0, :], max16[:, 1, :], ALU.max))
                    link(dve.transpose(max_rows[:, :].rearrange("p (a b) -> p a b", b=32),
                                       max8[:, :].unsqueeze(2).broadcast_to([P, TB, 32])))
                    dve.tensor_tensor(shifted_s[:, g % 2, :, :], s.rearrange("p (h s) -> p h s", h=HALVES),
                                      max_rows[:, :].unsqueeze(1).broadcast_to([P, HALVES, S]),
                                      ALU.subtract).then_inc(s_taken, 1)

                def back(g):
                    dve.wait_ge(e_done, GROUPS * b + g + 1)
                    link(dve.tensor_reduce(sum16[:, g % 2, :, :].rearrange("p h j -> p (h j)"),
                                           e[:, g % 2, :, :].rearrange("p h (a b) -> p (h a) b", b=32), AX.X, ALU.add,
                                           apply_transpose=True))
                    dve.tensor_tensor(sum8[:, g // 2 % 2, g % 2, :], sum16[:, g % 2, 0, :], sum16[:, g % 2, 1, :], ALU.add).then_inc(e_summed, 1)

                def octet(o):
                    dve.wait_ge(e_summed, GROUPS * b + 2 * o + 2)
                    link(dve.reciprocal(inv8[:, :, :].rearrange("p g j -> p (g j)"),
                                        sum8[:, o % 2, :, :].rearrange("p g j -> p (g j)")))
                    link(dve.transpose(inv_rows[:, :].rearrange("p (a g b) -> p a g b", g=2, b=16),
                                       inv8[:, :, :].rearrange("p g j -> p j g").unsqueeze(3)
                                       .broadcast_to([P, TB, 2, 16])))
                    dve.wait_ge(pv_done, GROUPS * b + 2 * o + 2)
                    dve.tensor_tensor(att[:, :], a_banks[two][o % 2][:, 0:S], inv_rows[:, :],
                                      ALU.mult).then_inc(a_taken, 1)
                    dve.wait_ge(a_taken, OCTS * b + o + 1)
                    dve.tensor_tensor(res[k][:, o, bass.ds(off, S)], res[k][:, o, bass.ds(off, S)], att[:, :],
                                      ALU.add).then_inc(res_done, 1)

                if slot == MEAN1 - 1:
                    dve.wait_ge(in_xq, 16 * b + 16)
                    octet_sums(x_q[:, :, :])
                if slot == MEAN1:
                    centre(x_q[:, :, :], 0)
                if slot == VAR1 - 1:
                    dve.wait_ge(ln_sq, 2 * b + 1)
                    octet_sums(xsq[:, :, :])
                if slot == VAR1:
                    normalise(0, 0.25)
                g = group_in(slot, 0)
                if g is not None:
                    front(g)
                g = group_in(slot, BACK)
                if g is not None:
                    back(g)
                g = group_in(slot, VALUES)
                if g is not None and g % 2 == 1:
                    octet(g // 2)
                if slot == SUM2:
                    dve.wait_ge(res_done, OCTS * b + OCTS)
                    octet_sums(stream)
                if slot == MEAN2:
                    centre(stream, 1)
                if slot == VAR2 - 1:
                    dve.wait_ge(ln_sq, 2 * b + 2)
                    octet_sums(xsq[:, :, :])
                if slot == VAR2:
                    normalise(1, 1.0)

            def links_before(slot):
                n = 0
                for s in range(slot):
                    n += (s in (MEAN1 - 1, VAR1 - 1, SUM2, VAR2 - 1)) + (LINKS_LN - 2) * (s in (VAR1, VAR2))
                    n += 3 * (group_in(s, 0) is not None) + (group_in(s, BACK) is not None)
                    n += 2 * ((group_in(s, VALUES) or 0) % 2)
                return n

            def dequantise(blk, i, slot):
                u, there = unit_ahead(blk, i, slot)
                if not there or slot % 3 == 2:
                    return
                n, kind = (STEPS * i + (slot + AHEAD) // 3), slot % 3
                if isinstance(n, int):
                    n = n % CHUNKS if n > CHUNKS else n
                w = w_raw[:, slot % STAGE, :, :]
                dve.wait_ge(in_w[slot % STAGE], 16 * (UNITS // STAGE * blk + SLOTS // STAGE * i
                                                      + (slot + AHEAD) // STAGE + 1))
                dve.tensor_tensor(w, w, scl[:, bass.ds(n, 1), kind, :].rearrange("p a o -> p (a o)")
                                  .unsqueeze(2).broadcast_to([P, 4, P]), ALU.mult).then_inc(wd_up_done, 1)

            def gate(n):
                dve.wait_ge(th_done, n + 1)
                dve.scalar_tensor_tensor(out=tg[:, :], in0=th[:, :], scalar=1.0, in1=g_ps[:, :],
                                         op0=ALU.add, op1=ALU.mult).then_inc(tg_done, 1)

            def hidden(n, j):
                dve.wait_ge(u_done, n + 1 + GU0)
                dve.wait_ge(tg_done, n + 1)
                dve.tensor_tensor(h[:, j % 2, :], tg[:, :], u_ps[:, :], ALU.mult).then_inc(h_done, 1)

            def ffn(blk, i, attend):
                for j in range(STEPS):
                    n = chunk(blk, i, j)
                    for third in range(3):
                        slot = 3 * j + third
                        if third == 1:
                            gate(n)
                        if third == 2:
                            hidden(n, j)
                        dequantise(blk, i, slot)
                        if attend:
                            attention(2 + i, slot, 1, S * i, False)

            def output(blk):
                dve.wait_ge(y_step, CHUNKS * (blk + 1) + Y0)
                for o in range(OCTS):
                    dve.tensor_tensor(res[blk][:, o, :], y_ps[o][:, :], res[blk][:, o, :],
                                      ALU.add).then_inc(y_taken, 1)

            dve.wait_ge(in_const, 48)
            dve.wait_ge(const_act, 2)
            dve.tensor_tensor(mask_split[T:P, :], mask_raw[T:P, :], mask_split[T:P, :],
                              ALU.subtract).then_inc(mask_done, 1)
            dve.tensor_scalar(scl[:, :, 2, :], scl[:, :, 2, :], 0.5, None, ALU.mult).then_inc(scl_done, 1)
            dve.wait_ge(in_xr[0], 32)
            with dve.Fori(0, 2) as b:
                for slot in range(SLOTS):
                    attention(b, slot, 0, S * b, True)
            dve.wait_ge(scl_done, 1)
            for u in range(AHEAD):
                dequantise(0, -1, SLOTS - AHEAD + u)
            dve.wait_ge(in_xr[1], 32)
            with dve.Fori(0, 2) as i:
                ffn(0, i, True)
            output(0)
            for i in range(2):
                ffn(1, i, False)
            output(1)

        @block.scalar
        def _(act):
            def attention(b, slot, k, off):
                if slot == MEAN1:
                    act.wait_ge(ln_xc, 2 * b + 1)
                    act.activation(xsq[:, :, :], xc[0][:, :, :], ACT.Square).then_inc(ln_sq, 1)
                g = group_in(slot, 0)
                if g is not None:
                    n = GROUPS * b + g
                    act.wait_ge(s_taken, n + 1)
                    if g >= 2:
                        act.wait_ge(pv_done, n - 1)
                    act.activation(e[:, g % 2, :, :], shifted_s[:, g % 2, :, :], ACT.Exp).then_inc(e_done, 1)
                if slot == MEAN2:
                    act.wait_ge(ln_xc, 2 * b + 2)
                    act.activation(xsq[:, :, :], xc[1][:, :, :], ACT.Square).then_inc(ln_sq, 1)
                if slot == VAR2:
                    act.wait_ge(ln_xn, 2 * b + 2)
                    act.activation(xn_hi[k][:, :, bass.ds(off, S)], xc[1][:, :, :], ACT.Copy).then_inc(xn_hi_done, 1)

            def split_unit(blk, i, slot):
                u, there = unit_ahead(blk, i, slot)
                if not there:
                    return
                n, kind = chunk(blk, i, 0) + (slot + AHEAD - RING) // 3, (slot + AHEAD - RING) % 3
                if not isinstance(i, int) or blk > 0:
                    act.wait_ge([g_done, u_done, y_step][kind], n + 1 + [GU0, GU0, Y0][kind])
                m = chunk(blk, i, 0) + (slot + AHEAD) // 3
                if slot % 3 == 2:
                    act.wait_ge(wd_down_done, m + 1)
                else:
                    act.wait_ge(wd_up_done, 2 * m + slot % 3 + 1)
                act.activation(w_hi[:, (slot + AHEAD) % RING, :, :], w_raw[:, slot % STAGE, :, :],
                               ACT.Copy).then_inc(w_hi_done, 1)

            def ffn(blk, i, attend):
                for j in range(STEPS):
                    n = chunk(blk, i, j)
                    for third in range(3):
                        slot = 3 * j + third
                        if third == 1:
                            act.wait_ge(g_done, n + 1 + GU0)
                            act.activation(th[:, :], g_ps[:, :], ACT.Tanh, scale=0.5).then_inc(th_done, 1)
                        if third == 2:
                            act.wait_ge(h_done, n + 1)
                            act.activation(h_hi[:, j % 2, :], h[:, j % 2, :], ACT.Copy).then_inc(h_hi_done, 1)
                        split_unit(blk, i, slot)
                        if attend:
                            attention(2 + i, slot, 1, S * i)

            act.wait_ge(in_const, 48)
            act.activation(sel_r[:, :, :], sel_raw[:, :, :], ACT.Copy).then_inc(const_act, 1)
            act.activation(mask_split[:, :], mask_raw[:, :], ACT.Copy).then_inc(const_act, 1)
            with act.Fori(0, 2) as b:
                for slot in range(SLOTS):
                    attention(b, slot, 0, S * b)
            for u in range(AHEAD):
                split_unit(0, -1, SLOTS - AHEAD + u)
            with act.Fori(0, 2) as i:
                ffn(0, i, True)
            for i in range(2):
                ffn(1, i, False)

        @block.gpsimd
        def _(pool):
            def low(dst, whole, high):
                return pool.tensor_tensor(dst, whole, high.bitcast(F32), ALU.subtract)

            def attention(b, slot, k, off):
                if slot == VAR2:
                    pool.wait_ge(xn_hi_done, b + 1)
                    low(xn_lo[k][:, :, bass.ds(off, S)], xc[1][:, :, :],
                        xn_hi[k][:, :, bass.ds(off, S)]).then_inc(xn_lo_done, 1)

            def dequantise(blk, i, slot):
                u, there = unit_ahead(blk, i, slot)
                if not there or slot % 3 != 2:
                    return
                n = STEPS * i + (slot + AHEAD) // 3
                if isinstance(n, int):
                    n = n % CHUNKS if n > CHUNKS else n
                w = w_raw[:, slot % STAGE, :, :]
                pool.wait_ge(in_w[slot % STAGE], 16 * (UNITS // STAGE * blk + SLOTS // STAGE * i
                                                       + (slot + AHEAD) // STAGE + 1))
                pool.tensor_tensor(w, w, scl[:, bass.ds(n, 1), 2, :].rearrange("p a o -> p (a o)")
                                   .unsqueeze(2).broadcast_to([P, 4, P]), ALU.mult).then_inc(wd_down_done, 1)

            def split_unit(blk, i, slot):
                u, there = unit_ahead(blk, i, slot)
                if not there:
                    return
                pool.wait_ge(w_hi_done, u + 1)
                low(w_lo[:, (slot + AHEAD) % RING, :, :], w_raw[:, slot % STAGE, :, :],
                    w_hi[:, (slot + AHEAD) % RING, :, :]).then_inc(w_lo_done, 1)

            def ffn(blk, i, attend):
                for j in range(STEPS):
                    n = chunk(blk, i, j)
                    for third in range(3):
                        slot = 3 * j + third
                        if third == 2:
                            pool.wait_ge(h_hi_done, n + 1)
                            low(h_lo[:, j % 2, :], h[:, j % 2, :], h_hi[:, j % 2, :]).then_inc(h_lo_done, 1)
                        dequantise(blk, i, slot)
                        split_unit(blk, i, slot)
                        if attend:
                            attention(2 + i, slot, 1, S * i)

            pool.memset(ones[:, :], 1.0 / D).then_inc(const_set, 1)
            pool.memset(zeros[:, :], 0.0).then_inc(xn_lo_done, XN0)
            with pool.Fori(0, 2) as b:
                for slot in range(SLOTS):
                    attention(b, slot, 0, S * b)
            pool.wait_ge(scl_done, 1)
            for u in range(AHEAD):
                dequantise(0, -1, SLOTS - AHEAD + u)
                split_unit(0, -1, SLOTS - AHEAD + u)
            with pool.Fori(0, 2) as i:
                ffn(0, i, True)
            for i in range(2):
                ffn(1, i, False)



def kernel(x, ctx_1024, mask_SxS2_ff0, L0_ffn_w1, L0_ffn_w1_scale, L0_ffn_w3, L0_ffn_w3_scale,
           L0_ffn_w2, L0_ffn_w2_scale):
    import concourse.bacc as bacc
    from concourse.bass_utils import run_bass_kernel_spmd

    x6 = np.asarray(x).reshape(B, S, OCTS, 2, 4, 16)
    c = np.asarray(ctx_1024).reshape(B, HALVES, 32, GROUPS, 16)
    kd = np.zeros((B, 2, 4, 16, GROUPS // 2, 2, HALVES, 4, 32), np.float32)
    vd = np.zeros((B, 4, 32, GROUPS // 2, 2, HALVES, 4, 2, 16), np.float32)
    ck = c.transpose(0, 4, 3, 1, 2).reshape(B, 16, GROUPS // 2, 2, HALVES, 32)
    cv = c.transpose(0, 2, 3, 1, 4).reshape(B, 32, GROUPS // 2, 2, HALVES, 16)
    for r in range(4):
        for two in range(2):
            kd[:, two, r, :, :, two, :, r, :] = ck[:, :, :, two]
            vd[:, r, :, :, two, :, r, two, :] = cv[:, :, :, two]
    mask_t = np.asarray(mask_SxS2_ff0).T
    sel = np.zeros((2, T, HALVES, 4, 32), np.float32)
    for t in range(T):
        sel[:, t, t // 32, :, t % 32] = 1.0

    def up_weights(w):
        w = np.asarray(w).reshape(CHUNKS, P, OCTS, 2, 4, 16)
        return w.transpose(0, 4, 3, 5, 2, 1).reshape(CHUNKS, P, OCTS, P)

    w2 = np.asarray(L0_ffn_w2).reshape(OCTS, 2, 4, 16, CHUNKS, P).transpose(4, 5, 0, 2, 1, 3)
    scales = np.stack([np.asarray(L0_ffn_w1_scale), np.asarray(L0_ffn_w3_scale),
                       np.asarray(L0_ffn_w2_scale).T], axis=1)
    scales = np.concatenate([scales, scales[:1]], axis=0)
    arrays = {
        "xq": x6.transpose(0, 3, 4, 5, 2, 1).reshape(B, P, OCTS, S),
        "xr": x6.transpose(0, 4, 3, 5, 2, 1).reshape(B, P, OCTS, S),
        "kd": kd.reshape(B, P, GROUPS * HALVES, P),
        "vd": vd.reshape(B, P, GROUPS * HALVES, P),
        "mask": np.concatenate([mask_t, mask_t], axis=0),
        "sel": sel.reshape(P, HALVES, P),
        "scales": np.broadcast_to(scales, (P,) + scales.shape),
        "w1": up_weights(L0_ffn_w1),
        "w3": up_weights(L0_ffn_w3),
        "w2": w2.reshape(CHUNKS, P, OCTS, P),
    }
    arrays = {name: np.ascontiguousarray(a) for name, a in arrays.items()}
    nc = bacc.Bacc("TRN2", target_bir_lowering=False, num_devices=1)
    args = {name: nc.dram_tensor(f"{name}_dram", a.shape, F32, kind="ExternalInput").ap()
            for name, a in arrays.items()}
    args["out"] = nc.dram_tensor("out_dram", (2, P, OCTS, BLOCK), F32, kind="ExternalOutput").ap()
    build(nc, **args)
    r = run_bass_kernel_spmd(nc, [{f"{name}_dram": a for name, a in arrays.items()}], core_ids=[0])
    got = r.results[0]["out_dram"].reshape(2, 4, 2, 16, OCTS, 2, S)
    return np.ascontiguousarray(got.transpose(0, 5, 6, 4, 2, 1, 3).reshape(B, S, D))
```

```python
from contextlib import ExitStack

import numpy as np

import concourse.bass as bass
from concourse import mybir

F32 = mybir.dt.float32
F32R = mybir.dt.float32r
I32 = mybir.dt.int32
ALU = mybir.AluOpType
ACT = mybir.ActivationFunctionType
AX = mybir.AxisListType

P = 128
B, S, T, D, INTER = 4, 256, 64, 512, 1792
OCTS = D // P
GROUPS = 8
HALVES = T // 32
TB = S // 32
BLOCK = 2 * S
CHUNKS = INTER // P
HALF = CHUNKS // 2
STEPS_A = 3 * HALF
STEPS = STEPS_A + CHUNKS
UNITS = 3 * STEPS
ROUND = 3
RING = 3 * ROUND
STAGE = 3
DVE_OCTS = 3
SUM_LEAD = 1
WARM_UP = (6, 8)
H_BUFS = ROUND
E_BUFS = 4
SEEDS = 3
EPS = 1e-5
SCALE = 0.25
RSQRT_MAGIC = float(0x5F3759DF)


class Schedule:

    def __init__(self, front, lead, back, values, octet, norms):
        self.front, self.lead, self.back, self.values, self.octet = front, lead, back, values, octet
        self.mean1, self.var1, self.mean2, self.var2 = norms

    def group(self, slot, shift):
        return self.front.index(slot - shift) if slot - shift in self.front else None


FIRST_SLOT = -18
PLAN = [Schedule([-15, -14, -13, -12, -10, -8, -7, -6], 1, 1, 2, 2, (-18, -17, -3, -2)),
        Schedule([-4, -3, -1, 1, 3, 5, 7, 9], 0, 1, 2, 2, (-12, -9, 15, 17)),
        Schedule([18, 20, 23, 24, 26, 28, 30, 31], 0, 1, 2, 2, (10, 12, 37, 39)),
        Schedule([36, 38, 40, 41, 43, 44, 46, 48], 0, 1, 2, 2, (29, 33, 53, 57))]
GATE, HIDDEN = 1, 2
FIRST_UNITS = [-10, -9, -8]


def norm(b, which):
    means = sorted([p.mean1 for p in PLAN] + [p.mean2 for p in PLAN])
    return means.index([PLAN[b].mean1, PLAN[b].mean2][which])


def before(b, slot, steps):
    return sum((s, c) < (slot, b) for s, c in steps)


def norm_sums(b, which):
    return 2 * sum(norm(c, w) < norm(b, which) for c in range(1, B) for w in range(2))


def chunk_of(n):
    return n % CHUNKS if n < STEPS_A else n - STEPS_A


def tokens_of(n):
    return (0, S) if n < HALF else (S, 2 * S) if CHUNKS <= n < STEPS_A else (0, 2 * S)


def build(nc, xq, xr, kd, vd, mask, sel, scales, w1, w3, w2, out):
    with ExitStack() as ctx:
        def sb(name, shape, dt=F32):
            return ctx.enter_context(nc.sbuf_tensor(name, shape, dt))

        def sem(name):
            return ctx.enter_context(nc.semaphore(name))

        x_q = [sb(f"x_q{k}", [P, OCTS, S]) for k in range(2)]
        res = [sb(f"res{k}", [P, OCTS, BLOCK]) for k in range(2)]
        xn_hi = [sb(f"xn_hi{k}", [P, OCTS, BLOCK], F32R) for k in range(2)]
        xn_lo = [sb(f"xn_lo{k}", [P, OCTS, BLOCK], F32R) for k in range(2)]
        keys = [sb(f"keys{k}", [P, GROUPS * HALVES, P]) for k in range(2)]
        values_ = [sb(f"values_{k}", [P, GROUPS * HALVES, P]) for k in range(2)]
        mask_raw = sb("mask_raw", [P, S])
        mask_split = sb("mask_split", [P, S], F32R)
        sel_raw = sb("sel_raw", [P, HALVES + 1, P])
        sel_r = sb("sel_r", [P, HALVES, P], F32R)
        ones = sb("ones", [P, P])
        zeros = sb("zeros", [P, BLOCK], mybir.dt.bfloat16)
        fsum = sb("fsum", [P, 2, S])
        fsum1 = sb("fsum1", [P, S])
        xc = [sb(f"xc{k}", [P, OCTS, S]) for k in range(3)]
        xsq = sb("xsq", [P, OCTS, S])
        var8 = sb("var8", [P, TB])
        shifted = sb("shifted", [P, TB], I32)
        rs8 = sb("rs8", [P, TB])
        newton = sb("newton", [P, TB])
        rstd = sb("rstd", [P, S])
        max16 = sb("max16", [P, HALVES, TB])
        max8 = sb("max8", [P, TB])
        max_rows = sb("max_rows", [P, S])
        max_pair = sb("max_pair", [P, 2, S])
        shifted_s = sb("shifted_s", [P, 2, HALVES, S])
        e = sb("e", [P, E_BUFS, HALVES, S])
        sum16 = sb("sum16", [P, 2, HALVES, TB])
        sum8 = sb("sum8", [P, 2, 2, TB])
        inv8 = sb("inv8", [P, 2, TB])
        inv_rows = sb("inv_rows", [P, S])
        att = sb("att", [P, 2, S])
        w_raw = sb("w_raw", [P, STAGE, 4, P])
        w_hi = sb("w_hi", [P, RING, 4, P], F32R)
        w_lo = sb("w_lo", [P, RING, 4, P], F32R)
        scl = sb("scl", [P, CHUNKS, 3, 4])
        th = sb("th", [P, BLOCK])
        tg = sb("tg", [P, BLOCK])
        h = sb("h", [P, H_BUFS, BLOCK])
        h_hi = sb("h_hi", [P, H_BUFS, BLOCK], F32R)
        h_lo = sb("h_lo", [P, H_BUFS, BLOCK], F32R)

        bank = [ctx.enter_context(nc.psum_tensor(f"bank{k}", [P, BLOCK], F32)) for k in range(8)]
        y_ps, g_ps, u_ps = bank[0:4], bank[4], bank[5]
        s_alone, a_alone, mean_alone = [g_ps, bank[0], bank[1]], [u_ps, bank[3]], bank[2][:, 0:S]
        s_beside, a_beside, mean_beside = bank[6], bank[7][:, 0:S], bank[6][:, 0:S]

        in_const = sem("in_const")
        in_scl = sem("in_scl")
        in_xq = [sem(f"in_xq{k}") for k in range(2)]
        in_xr = [sem(f"in_xr{k}") for k in range(B)]
        in_k = [sem(f"in_k{k}") for k in range(2)]
        in_v = [sem(f"in_v{k}") for k in range(2)]
        in_w = [sem(f"in_w{k}") for k in range(STAGE)]
        out_done = sem("out_done")
        const_set = sem("const_set")
        const_act = sem("const_act")
        mask_done = sem("mask_done")
        scl_done = sem("scl_done")
        dve_link = sem("dve_link")
        ln_sum = sem("ln_sum")
        ln_stat = sem("ln_stat")
        ln_xc = sem("ln_xc")
        ln_sq = sem("ln_sq")
        ln_rstd = sem("ln_rstd")
        ln_xn = sem("ln_xn")
        ln_xn_pool = sem("ln_xn_pool")
        s_done = sem("s_done")
        max_done = sem("max_done")
        s_shifted = sem("s_shifted")
        s_taken = sem("s_taken")
        e_done = sem("e_done")
        e_summed = sem("e_summed")
        pv_done = sem("pv_done")
        a_taken = sem("a_taken")
        res_done = sem("res_done")
        xn_hi_done = sem("xn_hi_done")
        xn_lo_done = sem("xn_lo_done")
        wd_gate_done = sem("wd_gate_done")
        wd_up_done = sem("wd_up_done")
        wd_down_done = sem("wd_down_done")
        w_hi_done = sem("w_hi_done")
        w_lo_done = sem("w_lo_done")
        g_done = sem("g_done")
        u_done = sem("u_done")
        y_step = sem("y_step")
        y_octet = sem("y_octet")
        th_done = sem("th_done")
        tg_done = sem("tg_done")
        h_done = sem("h_done")
        h_hi_done = sem("h_hi_done")
        h_lo_done = sem("h_lo_done")
        y_taken = sem("y_taken")


        block = ctx.enter_context(nc.Block())

        @block.sync
        def _(sp):
            def load_query(b):
                if b >= 2:
                    sp.wait_ge(ln_xc, norm(b - 2, 0) + 1)
                sp.dma_start(x_q[b % 2][:, :, :], xq[b, :, :, :]).then_inc(in_xq[b % 2], 16)

            def load_keys(b):
                if b >= 2:
                    sp.wait_ge(s_done, GROUPS * (b - 1))
                sp.dma_start(keys[b % 2][:, :, :], kd[b, :, :, :]).then_inc(in_k[b % 2], 16)

            def load_values(b):
                if b >= 2:
                    sp.wait_ge(pv_done, GROUPS * (b - 1))
                sp.dma_start(values_[b % 2][:, :, :], vd[b, :, :, :]).then_inc(in_v[b % 2], 16)

            def load_residual(b):
                sp.dma_start(res[b // 2][:, :, (b % 2) * S:(b % 2 + 1) * S], xr[b, :, :, :])\
                  .then_inc(in_xr[b], 16)

            def load_unit(u):
                if u >= STAGE:
                    sp.wait_ge(w_lo_done, u - STAGE + 1)
                sp.dma_start(w_raw[:, u % STAGE, :, :], [w1, w3, w2][u % 3][chunk_of(u // 3), :, :, :])\
                  .then_inc(in_w[u % STAGE], 16)

            def store_block(blk):
                for o in range(OCTS):
                    sp.wait_ge(y_taken, OCTS * blk + o + 1)
                    sp.dma_start(out[blk, :, o, :], res[blk][:, o, :]).then_inc(out_done, 16)

            load_query(0)
            sp.dma_start(mask_raw[:, :], mask).then_inc(in_const, 16)
            sp.dma_start(sel_raw[:, :, :], sel).then_inc(in_const, 16)
            load_keys(0)
            load_query(1)
            load_values(0)
            load_residual(0)
            load_keys(1)
            load_values(1)
            load_residual(1)
            sp.dma_start(scl[:, :, :, :], scales).then_inc(in_scl, 16)
            for u in range(STAGE):
                load_unit(u)
            load_residual(2)
            load_residual(3)
            load_query(2)
            load_keys(2)
            load_values(2)
            for u in range(STAGE, UNITS):
                load_unit(u)
                if u == PLAN[1].front[-1] + 4:
                    load_query(3)
                    load_keys(3)
                    load_values(3)
                if u == 3 * STEPS_A + 2 * RING:
                    store_block(0)
            store_block(1)
            sp.wait_ge(out_done, 16 * 2 * OCTS)

        @block.tensor
        def _(pe):
            def stat_alone(which, src):
                for o in range(OCTS):
                    last = pe.matmul(mean_alone, ones[:, :], src[:, o, :], start=(o == 0), stop=(o == OCTS - 1))
                last.then_inc(ln_stat, 1)

            def stat_beside(b, slot, count):
                pe.wait_ge(ln_sum, count)
                taken = before(b, slot, [(s, c) for c in range(1, B) for s in PLAN[c].front])
                if taken > 0:
                    pe.wait_ge(s_taken, taken)
                pe.matmul(mean_beside, ones[:, :], fsum1[:, :], start=True, stop=True).then_inc(ln_stat, 1)

            def statistics(b, slot, which, second):
                if b > 0:
                    stat_beside(b, slot, norm_sums(b, which) + 1 + second)
                elif second:
                    pe.wait_ge(ln_sq, norm(0, which) + 1)
                    stat_alone(which, xsq)
                elif which == 0:
                    pe.wait_ge(in_xq[0], 16)
                    stat_alone(which, x_q[0])
                else:
                    pe.wait_ge(res_done, OCTS)
                    stat_alone(which, res[0][:, :, 0:S])

            def scores(b, slot, g):
                n = GROUPS * b + g
                if g == 0:
                    if b == 0:
                        pe.wait_ge(const_act, 2)
                        pe.wait_ge(mask_done, 1)
                    pe.wait_ge(in_k[b % 2], 16 * (b // 2 + 1))
                    pe.wait_ge(ln_xn, norm(b, 0) + 1)
                    pe.wait_ge(ln_xn_pool, norm(b, 0) + 1)
                if b == 0 and g >= len(s_alone):
                    pe.wait_ge(e_done, n + 1 - len(s_alone))
                if n > GROUPS:
                    pe.wait_ge(s_taken, n - GROUPS)
                if b > 0:
                    pe.wait_ge(ln_xc, before(b, slot, [(s, c) for c in range(B) for s in (PLAN[c].mean1, PLAN[c].mean2)]))
                    pe.wait_ge(ln_rstd, before(b, slot, [(s, c) for c in range(B) for s in (PLAN[c].var1, PLAN[c].var2)]))
                dst = s_alone[g % len(s_alone)] if b == 0 else s_beside
                for half in range(HALVES):
                    d = dst[:, half * S:(half + 1) * S]
                    pe.matmul(d, sel_r[:, half, :], mask_split[:, :], start=(half == 0), stop=False,
                              skip_group_check=True)
                    last = pe.matmul(d, keys[b % 2][:, HALVES * g + half, :], xc[b % 2][:, g // 2, :], start=False,
                                     stop=(half == HALVES - 1), skip_group_check=True)
                last.then_inc(s_done, 1)

            def shift(g):
                pe.wait_ge(max_done, g + 1)
                pe.matmul(s_alone[g % len(s_alone)][:, :].rearrange("p (h s) -> p h s", h=HALVES),
                          sel_raw[:, HALVES, :], max_pair[:, g % 2, :].unsqueeze(1).broadcast_to([P, HALVES, S]),
                          start=False, stop=True, skip_group_check=True).then_inc(s_shifted, 1)

            def values(b, g):
                o = OCTS * b + g // 2
                if g == 0:
                    pe.wait_ge(in_v[b % 2], 16 * (b // 2 + 1))
                if g % 2 == 0 and (b > 0 or o >= 2):
                    pe.wait_ge(a_taken, o if b > 0 else o - 1)
                pe.wait_ge(e_done, GROUPS * b + g + 1)
                dst = a_beside if b > 0 else a_alone[o % 2][:, 0:S]
                for half in range(HALVES):
                    last = pe.matmul(dst, values_[b % 2][:, HALVES * g + half, :], e[:, g % E_BUFS, half, :],
                                     start=(g % 2 == 0 and half == 0), stop=(g % 2 == 1 and half == HALVES - 1))
                last.then_inc(pv_done, 1)

            def attention(slot):
                for b, plan in enumerate(PLAN):
                    if slot == plan.mean1:
                        statistics(b, slot, 0, 0)
                    if slot == plan.var1:
                        statistics(b, slot, 0, 1)
                    g = plan.group(slot, -plan.lead)
                    if g is not None:
                        scores(b, slot, g)
                    g = plan.group(slot, plan.values)
                    if g is not None:
                        values(b, g)
                    g = plan.group(slot, 0)
                    if g is not None and b == 0:
                        shift(g)
                    if slot == plan.mean2:
                        statistics(b, slot, 1, 0)
                    if slot == plan.var2:
                        statistics(b, slot, 1, 1)

            def hidden_half(n, like, kind):
                ring, blk, (first, last_) = (3 * like + kind) % RING, like // STEPS_A, tokens_of(like)
                if kind == 0 and like in (0, HALF, STEPS_A):
                    pe.wait_ge(xn_hi_done, [1, 2, 4][(0, HALF, STEPS_A).index(like)])
                pe.wait_ge(w_hi_done, 3 * n + kind + 1)
                pe.wait_ge(w_lo_done, 3 * n + kind + 1)
                if like > 0:
                    pe.wait_ge([tg_done, h_done][kind], n)
                dst = [g_ps, u_ps][kind][:, 0:last_ - first]
                for o in range(OCTS):
                    hi = xn_hi[blk][:, o, first:last_]
                    pe.matmul(dst, w_hi[:, ring, o, :], hi, start=(o == 0), stop=False)
                    pe.matmul(dst, w_lo[:, ring, o, :], hi, start=False, stop=False)
                if kind == 0 and like in (0, HALF, STEPS_A):
                    pe.wait_ge(xn_lo_done, [1, 2, 4][(0, HALF, STEPS_A).index(like)])
                for o in range(OCTS):
                    last = pe.matmul(dst, w_hi[:, ring, o, :], xn_lo[blk][:, o, first:last_], start=False,
                                     stop=(o == OCTS - 1))
                last.then_inc([g_done, u_done][kind], 1)

            def output_step(n, like):
                ring, (first, last_) = (3 * like + 2) % RING, tokens_of(like)
                pe.wait_ge(w_hi_done, 3 * n + 3)
                pe.wait_ge(w_lo_done, 3 * n + 3)
                pe.wait_ge(h_hi_done, n + 1)
                pe.wait_ge(h_lo_done, n + 1)
                hi, lo = [part[:, like % H_BUFS, 0:last_ - first] for part in (h_hi, h_lo)]
                for o in range(OCTS):
                    y = y_ps[o][:, first:last_]
                    pe.matmul(y, w_hi[:, ring, o, :], hi, start=False, stop=False, skip_group_check=True)
                    pe.matmul(y, w_hi[:, ring, o, :], lo, start=False, stop=False, skip_group_check=True)
                    last = pe.matmul(y, w_lo[:, ring, o, :], hi, start=False, stop=False, skip_group_check=True)
                    if like in (STEPS_A - 1, STEPS - 1):
                        last.then_inc(y_octet, 1)
                if like not in (STEPS_A - 1, STEPS - 1):
                    last.then_inc(y_step, 1)

            def seed():
                for o in range(OCTS):
                    pe.matmul(y_ps[o][:, :], zeros[:, 0:P], zeros[:, :], start=True, stop=True,
                              skip_group_check=True)

            def step(n, like):
                hidden_half(n, like, 0)
                if like <= STEPS_A:
                    attention(3 * like)
                hidden_half(n, like, 1)
                if like <= STEPS_A:
                    attention(3 * like + 1)
                if like > 0:
                    output_step(n - 1, like - 1)
                if like == 0:
                    seed()
                if like <= STEPS_A:
                    attention(3 * like + 2)

            pe.wait_ge(const_set, 2)
            for slot in range(FIRST_SLOT, 0):
                if slot in (PLAN[0].mean1, PLAN[0].var1):
                    for _ in range(WARM_UP[slot == PLAN[0].var1]):
                        pe.matmul(bank[3][:, :], zeros[:, 0:P], zeros[:, :], start=True, stop=True)
                attention(slot)
            for n in range(STEPS_A + 1):
                step(n, n)
            pe.wait_ge(y_taken, OCTS)
            seed()
            with pe.Fori(0, (CHUNKS - 2) // ROUND) as r:
                for k in range(ROUND):
                    step(STEPS_A + 1 + ROUND * r + k, STEPS_A + 1 + k)
            step(STEPS - 1, STEPS - 1)
            output_step(STEPS - 1, STEPS - 1)

        @block.vector
        def _(dve):
            links = [0]

            def after(ins):
                links[0] += 1
                ins.then_inc(dve_link, 1)
                return links[0]

            def link(ins):
                dve.wait_ge(dve_link, after(ins))

            def octet_sums(src):
                link(dve.tensor_tensor(fsum[:, :, :], src[:, 0:2, :], src[:, 2:4, :], ALU.add))
                dve.tensor_tensor(fsum1[:, :], fsum[:, 0, :], fsum[:, 1, :], ALU.add).then_inc(ln_sum, 1)

            def centre(b, which, dst, src):
                dve.wait_ge(ln_stat, 2 * norm(b, which) + 1)
                if which == 1 and b > 0:
                    dve.wait_ge(xn_lo_done, b)
                mean = mean_beside if b > 0 else mean_alone
                dve.tensor_tensor(dst[:, :, :], src, mean.unsqueeze(1).broadcast_to([P, OCTS, S]),
                                  ALU.subtract).then_inc(ln_xc, 1)

            def normalise(b, which, dst):
                k = norm(b, which)
                dve.wait_ge(ln_stat, 2 * k + 2)
                var = mean_beside if b > 0 else mean_alone
                link(dve.tensor_reduce(var8[:, :], var.rearrange("p (a b) -> p a b", b=32), AX.X, ALU.max,
                                       apply_transpose=True))
                link(dve.tensor_scalar(var8[:, :], var8[:, :], EPS, None, ALU.add))
                link(dve.tensor_scalar(shifted[:, :], var8[:, :].bitcast(I32), 1, None, ALU.logical_shift_right))
                link(dve.tensor_scalar(rs8[:, :].bitcast(I32), shifted[:, :], -1.0, RSQRT_MAGIC,
                                       ALU.mult, ALU.add))
                for _ in range(SEEDS):
                    link(dve.scalar_tensor_tensor(out=newton[:, :], in0=rs8[:, :], scalar=-0.5, in1=rs8[:, :],
                                                  op0=ALU.mult, op1=ALU.mult))
                    link(dve.tensor_tensor(newton[:, :], newton[:, :], var8[:, :], ALU.mult))
                    link(dve.scalar_tensor_tensor(out=rs8[:, :], in0=newton[:, :], scalar=1.5, in1=rs8[:, :],
                                                  op0=ALU.add, op1=ALU.mult))
                if k > 0:
                    dve.wait_ge(ln_xn_pool, k)
                dve.transpose(rstd[:, :].rearrange("p (a b) -> p a b", b=32),
                              rs8[:, :].unsqueeze(2).broadcast_to([P, TB, 32])).then_inc(ln_rstd, 1)
                dve.wait_ge(ln_rstd, k + 1)
                dve.tensor_tensor(dst[:, 0:DVE_OCTS, :], dst[:, 0:DVE_OCTS, :],
                                  rstd[:, :].unsqueeze(1).broadcast_to([P, DVE_OCTS, S]), ALU.mult).then_inc(ln_xn, 1)

            def sums(b, g):
                dve.wait_ge(e_done, GROUPS * b + g + 1)
                return after(dve.tensor_reduce(sum16[:, g % 2, :, :].rearrange("p h j -> p (h j)"),
                                               e[:, g % E_BUFS, :, :].rearrange("p h (a b) -> p (h a) b", b=32), AX.X,
                                               ALU.add, apply_transpose=True))

            def add_halves(g):
                dve.tensor_tensor(sum8[:, g // 2 % 2, g % 2, :], sum16[:, g % 2, 0, :], sum16[:, g % 2, 1, :],
                                  ALU.add).then_inc(e_summed, 1)

            def softmax_steps(b, gf, gb):
                if gf is not None:
                    n = GROUPS * b + gf
                    dst = s_beside if b > 0 else s_alone[gf % len(s_alone)]
                    dve.wait_ge(s_done, n + 1)
                    reduced = after(dve.tensor_reduce(max16[:, :, :].rearrange("p h j -> p (h j)"),
                                                      dst.rearrange("p (a b) -> p a b", b=32), AX.X, ALU.max,
                                                      apply_transpose=True))
                if gb is not None:
                    summed = sums(b, gb)
                if gf is not None:
                    dve.wait_ge(dve_link, reduced)
                    if n > 0:
                        dve.wait_ge(max_done, min(n, GROUPS))
                    reduced = after(dve.tensor_tensor(max8[:, :], max16[:, 0, :], max16[:, 1, :], ALU.max))
                if gb is not None:
                    dve.wait_ge(dve_link, summed)
                    add_halves(gb)
                if gf is not None:
                    dve.wait_ge(dve_link, reduced)
                    wide = max8[:, :].unsqueeze(2).broadcast_to([P, TB, 32])
                    if b == 0:
                        if n >= 2:
                            dve.wait_ge(s_shifted, n - 1)
                        dve.transpose(max_pair[:, n % 2, :].rearrange("p (a b) -> p a b", b=32),
                                      wide).then_inc(max_done, 1)
                    else:
                        link(dve.transpose(max_rows[:, :].rearrange("p (a b) -> p a b", b=32), wide))
                        if n >= GROUPS + 2:
                            dve.wait_ge(e_done, n - 1)
                        dve.tensor_tensor(shifted_s[:, n % 2, :, :], dst.rearrange("p (h s) -> p h s", h=HALVES),
                                          max_rows[:, :].unsqueeze(1).broadcast_to([P, HALVES, S]),
                                          ALU.subtract).then_inc(s_taken, 1)

            def octet(b, o):
                n = OCTS * b + o
                dve.wait_ge(e_summed, 2 * n + 2)
                link(dve.reciprocal(inv8[:, :, :].rearrange("p g j -> p (g j)"),
                                    sum8[:, o % 2, :, :].rearrange("p g j -> p (g j)")))
                link(dve.transpose(inv_rows[:, :].rearrange("p (a g b) -> p a g b", g=2, b=16),
                                   inv8[:, :, :].rearrange("p g j -> p j g").unsqueeze(3)
                                   .broadcast_to([P, TB, 2, 16])))
                dve.wait_ge(pv_done, 2 * n + 2)
                if n >= 2:
                    dve.wait_ge(res_done, n - 1)
                dve.tensor_tensor(att[:, o % 2, :], a_beside if b > 0 else a_alone[o % 2][:, 0:S],
                                  inv_rows[:, :], ALU.mult).then_inc(a_taken, 1)

            def attention(slot):
                for b, plan in enumerate(PLAN):
                    stream = res[b // 2][:, :, b % 2 * S:b % 2 * S + S]
                    if slot == plan.mean1 - SUM_LEAD and b > 0:
                        dve.wait_ge(in_xq[b % 2], 16 * (b // 2 + 1))
                        octet_sums(x_q[b % 2])
                    if slot == plan.mean1:
                        centre(b, 0, xc[b % 2], x_q[b % 2][:, :, :])
                    if slot == plan.var1 - SUM_LEAD and b > 0:
                        dve.wait_ge(ln_sq, norm(b, 0) + 1)
                        octet_sums(xsq)
                    if slot == plan.var1:
                        normalise(b, 0, xc[b % 2])
                    softmax_steps(b, plan.group(slot, 0), plan.group(slot, plan.back))
                    g = plan.group(slot, plan.octet)
                    if g is not None and g % 2 == 1:
                        octet(b, g // 2)
                    if slot == plan.mean2 - SUM_LEAD and b > 0:
                        dve.wait_ge(res_done, OCTS * (b + 1))
                        octet_sums(stream)
                    if slot == plan.mean2:
                        centre(b, 1, xc[2], stream)
                    if slot == plan.var2 - SUM_LEAD and b > 0:
                        dve.wait_ge(ln_sq, norm(b, 1) + 1)
                        octet_sums(xsq)
                    if slot == plan.var2:
                        normalise(b, 1, xc[2])

            def dequantise(n, like, kind):
                if kind != 0 or like >= STEPS:
                    return
                w = w_raw[:, kind, :, :]
                chunk = chunk_of(n) if isinstance(n, int) else n - STEPS_A
                dve.wait_ge(in_w[kind], 16 * (n + 1))
                dve.tensor_tensor(w, w, scl[:, bass.ds(chunk, 1), kind, :].rearrange("p a o -> p (a o)")
                                  .unsqueeze(2).broadcast_to([P, 4, P]), ALU.mult).then_inc(wd_gate_done, 1)

            def gate(n, width):
                dve.wait_ge(th_done, n + 1)
                dve.scalar_tensor_tensor(out=tg[:, 0:width], in0=th[:, 0:width], scalar=1.0, in1=g_ps[:, 0:width],
                                         op0=ALU.add, op1=ALU.mult).then_inc(tg_done, 1)

            def hidden(n, like, width):
                dve.wait_ge(u_done, n + 1)
                dve.wait_ge(tg_done, n + 1)
                dve.tensor_tensor(h[:, like % H_BUFS, 0:width], tg[:, 0:width], u_ps[:, 0:width],
                                  ALU.mult).then_inc(h_done, 1)

            def step(n, like):
                width = tokens_of(like)[1] - tokens_of(like)[0]
                for third in range(3):
                    if third == GATE:
                        gate(n, width)
                    if third == HIDDEN:
                        hidden(n, like, width)
                    dequantise(n + 1, like + 1, third)
                    if like <= STEPS_A:
                        attention(3 * like + third)

            def output(blk):
                for o in range(OCTS):
                    dve.wait_ge(y_octet, OCTS * blk + o + 1)
                    dve.tensor_tensor(res[blk][:, o, :], y_ps[o][:, :], res[blk][:, o, :],
                                      ALU.add).then_inc(y_taken, 1)

            for slot in range(FIRST_SLOT, 0):
                attention(slot)
                if slot == PLAN[0].mean1 + 1:
                    dve.wait_ge(const_act, 2)
                    dve.tensor_tensor(mask_split[T:P, :], mask_raw[T:P, :], mask_split[T:P, :],
                                      ALU.subtract).then_inc(mask_done, 1)
                if slot in FIRST_UNITS:
                    if slot == FIRST_UNITS[0]:
                        dve.wait_ge(in_scl, 16)
                    dequantise(0, 0, FIRST_UNITS.index(slot))
            for n in range(STEPS_A + 1):
                step(n, n)
            output(0)
            with dve.Fori(0, (CHUNKS - 2) // ROUND) as r:
                for k in range(ROUND):
                    step(STEPS_A + 1 + ROUND * r + k, STEPS_A + 1 + k)
            step(STEPS - 1, STEPS - 1)
            output(1)

        @block.scalar
        def _(act):
            def attention(slot):
                for b, plan in enumerate(PLAN):
                    if slot == plan.mean1:
                        act.wait_ge(ln_xc, norm(b, 0) + 1)
                        act.activation(xsq[:, :, :], xc[b % 2][:, :, :], ACT.Square).then_inc(ln_sq, 1)
                    g = plan.group(slot, 0)
                    if g is not None:
                        n = GROUPS * b + g
                        if n >= E_BUFS:
                            act.wait_ge(pv_done, n + 1 - E_BUFS)
                            act.wait_ge(e_summed, n + 1 - E_BUFS)
                        if b == 0:
                            act.wait_ge(s_shifted, n + 1)
                            src = s_alone[g % len(s_alone)].rearrange("p (h s) -> p h s", h=HALVES)
                        else:
                            act.wait_ge(s_taken, n - GROUPS + 1)
                            src = shifted_s[:, g % 2, :, :]
                        act.activation(e[:, g % E_BUFS, :, :], src, ACT.Exp, scale=SCALE).then_inc(e_done, 1)
                    if slot == plan.mean2:
                        act.wait_ge(ln_xc, norm(b, 1) + 1)
                        act.activation(xsq[:, :, :], xc[2][:, :, :], ACT.Square).then_inc(ln_sq, 1)
                    if slot == plan.var2:
                        act.wait_ge(ln_xn, norm(b, 1) + 1)
                        act.wait_ge(ln_xn_pool, norm(b, 1) + 1)
                        act.activation(xn_hi[b // 2][:, :, b % 2 * S:b % 2 * S + S], xc[2][:, :, :],
                                       ACT.Copy).then_inc(xn_hi_done, 1)

            def dequantise(n, like):
                chunk = chunk_of(n) if isinstance(n, int) else n - STEPS_A
                act.wait_ge(in_w[1], 16 * (n + 1))
                for o in range(OCTS):
                    act.activation(w_raw[:, 1, o, :], w_raw[:, 1, o, :], ACT.Copy,
                                   scale=scl[:, bass.ds(chunk, 1), 1, o]).then_inc(wd_up_done, 1)

            def split_unit(n, like, kind):
                if like >= STEPS:
                    return
                if like >= ROUND:
                    if kind == 2 and like - ROUND == STEPS_A - 1:
                        act.wait_ge(y_octet, OCTS)
                    else:
                        act.wait_ge([g_done, u_done, y_step][kind],
                                    n - ROUND + 1 - (kind == 2 and like - ROUND >= STEPS_A))
                if kind == 1:
                    dequantise(n, like)
                act.wait_ge([wd_gate_done, wd_up_done, wd_down_done][kind], [n + 1, OCTS * (n + 1), n + 1][kind])
                act.activation(w_hi[:, (3 * like + kind) % RING, :, :], w_raw[:, kind, :, :],
                               ACT.Copy).then_inc(w_hi_done, 1)

            def step(n, like):
                width = tokens_of(like)[1] - tokens_of(like)[0]
                for third in range(3):
                    if third == GATE:
                        act.wait_ge(g_done, n + 1)
                        act.activation(th[:, 0:width], g_ps[:, 0:width], ACT.Tanh, scale=0.5).then_inc(th_done, 1)
                    if third == HIDDEN:
                        act.wait_ge(h_done, n + 1)
                        act.activation(h_hi[:, like % H_BUFS, 0:width], h[:, like % H_BUFS, 0:width],
                                       ACT.Copy).then_inc(h_hi_done, 1)
                    split_unit(n + 1, like + 1, third)
                    if like <= STEPS_A:
                        attention(3 * like + third)

            act.wait_ge(in_const, 32)
            act.activation(sel_r[:, :, :], sel_raw[:, 0:HALVES, :], ACT.Copy).then_inc(const_act, 1)
            act.activation(mask_split[:, :], mask_raw[:, :], ACT.Copy).then_inc(const_act, 1)
            for slot in range(FIRST_SLOT, 0):
                attention(slot)
                if slot in FIRST_UNITS:
                    split_unit(0, 0, FIRST_UNITS.index(slot))
            for n in range(STEPS_A + 1):
                step(n, n)
            with act.Fori(0, (CHUNKS - 2) // ROUND) as r:
                for k in range(ROUND):
                    step(STEPS_A + 1 + ROUND * r + k, STEPS_A + 1 + k)
            step(STEPS - 1, STEPS - 1)

        @block.gpsimd
        def _(pool):
            def low(dst, whole, high):
                return pool.tensor_tensor(dst, whole, high.bitcast(F32), ALU.subtract)

            def normalise(b, which, dst):
                pool.wait_ge(ln_rstd, norm(b, which) + 1)
                pool.tensor_tensor(dst[:, DVE_OCTS:OCTS, :], dst[:, DVE_OCTS:OCTS, :],
                                   rstd[:, :].unsqueeze(1).broadcast_to([P, OCTS - DVE_OCTS, S]), ALU.mult).then_inc(ln_xn_pool, 1)

            def attention(slot):
                for b, plan in enumerate(PLAN):
                    off = b % 2 * S
                    if slot == plan.var1:
                        normalise(b, 0, xc[b % 2])
                    g = plan.group(slot, plan.octet)
                    if g is not None and g % 2 == 1:
                        o = g // 2
                        if o == 0:
                            pool.wait_ge(in_xr[b], 16)
                        pool.wait_ge(a_taken, OCTS * b + o + 1)
                        stream = res[b // 2][:, o, off:off + S]
                        pool.tensor_tensor(stream, stream, att[:, o % 2, :], ALU.add).then_inc(res_done, 1)
                    if slot == plan.var2:
                        normalise(b, 1, xc[2])
                        pool.wait_ge(xn_hi_done, b + 1)
                        low(xn_lo[b // 2][:, :, off:off + S], xc[2][:, :, :],
                            xn_hi[b // 2][:, :, off:off + S]).then_inc(xn_lo_done, 1)

            def dequantise(n, like):
                w = w_raw[:, 2, :, :]
                chunk = chunk_of(n) if isinstance(n, int) else n - STEPS_A
                pool.wait_ge(in_w[2], 16 * (n + 1))
                pool.tensor_tensor(w, w, scl[:, bass.ds(chunk, 1), 2, :].rearrange("p a o -> p (a o)")
                                   .unsqueeze(2).broadcast_to([P, 4, P]), ALU.mult).then_inc(wd_down_done, 1)

            def split_unit(n, like, kind):
                if like >= STEPS:
                    return
                if kind == 2:
                    dequantise(n, like)
                pool.wait_ge(w_hi_done, 3 * n + kind + 1)
                ring = (3 * like + kind) % RING
                low(w_lo[:, ring, :, :], w_raw[:, kind, :, :], w_hi[:, ring, :, :]).then_inc(w_lo_done, 1)

            def step(n, like):
                width = tokens_of(like)[1] - tokens_of(like)[0]
                for third in range(3):
                    if third == HIDDEN:
                        pool.wait_ge(h_hi_done, n + 1)
                        low(h_lo[:, like % H_BUFS, 0:width], h[:, like % H_BUFS, 0:width],
                            h_hi[:, like % H_BUFS, 0:width]).then_inc(h_lo_done, 1)
                    split_unit(n + 1, like + 1, third)
                    if like <= STEPS_A:
                        attention(3 * like + third)

            pool.memset(ones[:, :], 1.0 / D).then_inc(const_set, 1)
            pool.memset(zeros[:, :], 0.0).then_inc(const_set, 1)
            for slot in range(FIRST_SLOT, 0):
                attention(slot)
                if slot in FIRST_UNITS:
                    if slot == FIRST_UNITS[0]:
                        pool.wait_ge(in_scl, 16)
                        pool.tensor_scalar(scl[:, :, 2, :], scl[:, :, 2, :], 0.5, None, ALU.mult).then_inc(scl_done, 1)
                        pool.wait_ge(scl_done, 1)
                    split_unit(0, 0, FIRST_UNITS.index(slot))
            for n in range(STEPS_A + 1):
                step(n, n)
            with pool.Fori(0, (CHUNKS - 2) // ROUND) as r:
                for k in range(ROUND):
                    step(STEPS_A + 1 + ROUND * r + k, STEPS_A + 1 + k)
            step(STEPS - 1, STEPS - 1)



def kernel(x, ctx_1024, mask_SxS2_ff0, L0_ffn_w1, L0_ffn_w1_scale, L0_ffn_w3, L0_ffn_w3_scale,
           L0_ffn_w2, L0_ffn_w2_scale):
    import concourse.bacc as bacc
    from concourse.bass_utils import run_bass_kernel_spmd

    x6 = np.asarray(x).reshape(B, S, OCTS, 2, 4, 16)
    c = np.asarray(ctx_1024).reshape(B, HALVES, 32, GROUPS, 16)
    kd = np.zeros((B, 2, 4, 16, GROUPS // 2, 2, HALVES, 4, 32), np.float32)
    vd = np.zeros((B, 4, 32, GROUPS // 2, 2, HALVES, 4, 2, 16), np.float32)
    ck = c.transpose(0, 4, 3, 1, 2).reshape(B, 16, GROUPS // 2, 2, HALVES, 32)
    cv = c.transpose(0, 2, 3, 1, 4).reshape(B, 32, GROUPS // 2, 2, HALVES, 16)
    for r in range(4):
        for two in range(2):
            kd[:, two, r, :, :, two, :, r, :] = ck[:, :, :, two]
            vd[:, r, :, :, two, :, r, two, :] = cv[:, :, :, two]
    mask_t = np.asarray(mask_SxS2_ff0).T
    sel = np.zeros((2, T, HALVES + 1, 4, 32), np.float32)
    for t in range(T):
        sel[:, t, t // 32, :, t % 32] = 1.0 / SCALE
    for row in range(P):
        sel[row // T, row % T, HALVES, row // 32, row % 32] = -1.0

    def up_weights(w):
        w = np.asarray(w).reshape(CHUNKS, P, OCTS, 2, 4, 16)
        return w.transpose(0, 4, 3, 5, 2, 1).reshape(CHUNKS, P, OCTS, P)

    w2 = np.asarray(L0_ffn_w2).reshape(OCTS, 2, 4, 16, CHUNKS, P).transpose(4, 5, 0, 2, 1, 3)
    scales = np.stack([np.asarray(L0_ffn_w1_scale), np.asarray(L0_ffn_w3_scale),
                       np.asarray(L0_ffn_w2_scale).T], axis=1)
    arrays = {
        "xq": x6.transpose(0, 3, 4, 5, 2, 1).reshape(B, P, OCTS, S),
        "xr": x6.transpose(0, 4, 3, 5, 2, 1).reshape(B, P, OCTS, S),
        "kd": kd.reshape(B, P, GROUPS * HALVES, P),
        "vd": vd.reshape(B, P, GROUPS * HALVES, P),
        "mask": np.concatenate([mask_t, mask_t], axis=0),
        "sel": sel.reshape(P, HALVES + 1, P),
        "scales": np.broadcast_to(scales, (P,) + scales.shape),
        "w1": up_weights(L0_ffn_w1),
        "w3": up_weights(L0_ffn_w3),
        "w2": w2.reshape(CHUNKS, P, OCTS, P),
    }
    arrays = {name: np.ascontiguousarray(a) for name, a in arrays.items()}
    nc = bacc.Bacc("TRN2", target_bir_lowering=False, num_devices=1)
    args = {name: nc.dram_tensor(f"{name}_dram", a.shape, F32, kind="ExternalInput").ap()
            for name, a in arrays.items()}
    args["out"] = nc.dram_tensor("out_dram", (2, P, OCTS, BLOCK), F32, kind="ExternalOutput").ap()
    build(nc, **args)
    r = run_bass_kernel_spmd(nc, [{f"{name}_dram": a for name, a in arrays.items()}], core_ids=[0])
    got = r.results[0]["out_dram"].reshape(2, 4, 2, 16, OCTS, 2, S)
    return np.ascontiguousarray(got.transpose(0, 5, 6, 4, 2, 1, 3).reshape(B, S, D))
```
